# Optimizing a Trainium2 kernel written in Bass

```python
import numpy as np
import jax
import jax.numpy as jnp

def _softmax(x, axis=-1):
    return jax.nn.softmax(x, axis=axis)

def _gelu(x):
    return jax.nn.gelu(x, approximate=True)

def _silu(x):
    return jax.nn.silu(x)

def _sigmoid(x):
    return jax.nn.sigmoid(x)

def _layernorm(x, axis=-1, eps=1e-05):
    m = jnp.mean(x, axis=axis, keepdims=True)
    v = jnp.var(x, axis=axis, keepdims=True)
    return (x - m) / jnp.sqrt(v + eps)

def _scatter_add(tgt, idx, src, axis=0):
    return tgt.at[idx].add(src)

def _segment_sum(src, seg, n):
    return jax.ops.segment_sum(src, seg, n)
kernel_name = 'mk_gnn_preln_d2_gnn_r8_ddc193'

def setup_inputs(seed: int=0):
    np.random.seed(seed)
    _w = jnp.asarray

    def _rec_inputs():
        import jax
        import jax.numpy as jnp
        _gk = jax.random.key(seed)
        x = 4.987e-05 + 0.125 * jax.random.normal(jax.random.fold_in(_gk, 1), (12500, 64), jnp.float32)
        src = jax.random.randint(jax.random.fold_in(_gk, 2), (400000,), 0, 12500, jnp.int32)
        dst = jnp.minimum((12500 * jax.random.uniform(jax.random.fold_in(_gk, 3), (400000,)) ** 2.0).astype(jnp.int32), 99999)
        _o = jnp.argsort(dst, stable=True)
        src = src[_o]
        dst = dst[_o]
        edge_attr_64 = jax.random.uniform(jax.random.fold_in(_gk, 12), (400000, 64), jnp.float32, 0.0, 1)
        edge_type_16 = jax.random.randint(jax.random.fold_in(_gk, 14), (400000,), 0, 16, jnp.int32)
        return (x, src, dst, edge_attr_64, edge_type_16)
    x, src, dst, edge_attr_64, edge_type_16 = _rec_inputs()

    def _L0_gnn_setup():
        import jax, jax.numpy as jnp
        import numpy as np
        NUM_NODES = 12500
        NUM_RELATIONS = 16
        HIDDEN = 64
        NUM_LAYERS = 3
        NUM_EDGES = 200000

        def _rgcn_layer(x, src, dst, et, Wr, Wroot, b):
            N, d = x.shape
            R = Wr.shape[0]
            xW = jnp.einsum('nd,rdh->rnh', x, Wr)
            m = xW[et, src]
            seg = dst * R + et
            counts = jax.ops.segment_sum(jnp.ones((m.shape[0],), dtype=x.dtype), seg, num_segments=N * R)
            norm = 1.0 / jnp.maximum(counts, 1.0)
            m = m * norm[seg][:, None]
            agg = jax.ops.segment_sum(m, dst, num_segments=N)
            return agg + x @ Wroot + b
        key = jax.random.key(seed)
        ks = jax.random.split(key, 6)
        edge_index = jax.random.randint(ks[0], (2, NUM_EDGES), 0, NUM_NODES, dtype=jnp.int64 if jax.config.jax_enable_x64 else jnp.int32)
        edge_type = jax.random.randint(ks[1], (NUM_EDGES,), 0, NUM_RELATIONS, dtype=edge_index.dtype)
        scale = 1.0 / np.sqrt(HIDDEN)
        node_emb = jax.random.normal(ks[2], (NUM_NODES, HIDDEN), dtype=jnp.float32) * scale
        W = jax.random.normal(ks[3], (NUM_LAYERS, NUM_RELATIONS, HIDDEN, HIDDEN), dtype=jnp.float32) * scale
        W_root = jax.random.normal(ks[4], (NUM_LAYERS, HIDDEN, HIDDEN), dtype=jnp.float32) * scale
        bias = jnp.zeros((NUM_LAYERS, HIDDEN), dtype=jnp.float32)
        return {'edge_index': edge_index, 'edge_type': edge_type, 'node_emb': node_emb, 'W': W, 'W_root': W_root, 'bias': bias}
    _L0_gnn_all = _L0_gnn_setup()
    _L0_gnn_in = {k: v for k, v in _L0_gnn_all.items() if k in ('W', 'W_root', 'bias')}
    del _L0_gnn_all

    def _L1_gnn_setup():
        import jax, jax.numpy as jnp
        import numpy as np
        N, E, D, K = (12500, 156250, 64, 64)
        key = jax.random.key(seed)
        ks = jax.random.split(key, 12)
        s = 1.0 / np.sqrt(D)
        return {'x': jax.random.normal(ks[0], (N, D), dtype=jnp.float32), 'i': jax.random.randint(ks[1], (E,), 0, N), 'j': jax.random.randint(ks[2], (E,), 0, N), 'rbf': jax.random.uniform(ks[3], (E, K), dtype=jnp.float32), 'Wf1': jax.random.uniform(ks[4], (D, K), jnp.float32, -s, s), 'bf1': jax.random.uniform(ks[5], (D,), jnp.float32, -s, s), 'Wf2': jax.random.uniform(ks[6], (D, D), jnp.float32, -s, s), 'bf2': jax.random.uniform(ks[7], (D,), jnp.float32, -s, s), 'Wl': jax.random.uniform(ks[8], (D, D), jnp.float32, -s, s), 'bl': jax.random.uniform(ks[9], (D,), jnp.float32, -s, s), 'gamma': jnp.ones((D,), jnp.float32), 'beta': jnp.zeros((D,), jnp.float32)}
    _L1_gnn_all = _L1_gnn_setup()
    _L1_gnn_in = {k: v for k, v in _L1_gnn_all.items() if k in ('Wf1', 'bf1', 'Wf2', 'bf2', 'Wl', 'bl', 'gamma', 'beta')}
    del _L1_gnn_all
    return {'x': x, 'src': src, 'dst': dst, 'edge_attr_64': edge_attr_64, 'edge_type_16': edge_type_16, 'L0_gnn_W': _L0_gnn_in['W'], 'L0_gnn_W_root': _L0_gnn_in['W_root'], 'L0_gnn_bias': _L0_gnn_in['bias'], 'L1_gnn_Wf1': _L1_gnn_in['Wf1'], 'L1_gnn_bf1': _L1_gnn_in['bf1'], 'L1_gnn_Wf2': _L1_gnn_in['Wf2'], 'L1_gnn_bf2': _L1_gnn_in['bf2'], 'L1_gnn_Wl': _L1_gnn_in['Wl'], 'L1_gnn_bl': _L1_gnn_in['bl'], 'L1_gnn_gamma': _L1_gnn_in['gamma'], 'L1_gnn_beta': _L1_gnn_in['beta']}

def reference(x, src, dst, edge_attr_64, edge_type_16, L0_gnn_W, L0_gnn_W_root, L0_gnn_bias, L1_gnn_Wf1, L1_gnn_bf1, L1_gnn_Wf2, L1_gnn_bf2, L1_gnn_Wl, L1_gnn_bl, L1_gnn_gamma, L1_gnn_beta):
    import jax
    import jax.numpy as jnp

    def _L0_gnn_ref(edge_index, edge_type, node_emb, W, W_root, bias):
        import jax, jax.numpy as jnp
        import numpy as np
        NUM_NODES = 12500
        NUM_RELATIONS = 16
        HIDDEN = 64
        NUM_LAYERS = 3
        NUM_EDGES = 200000

        def _rgcn_layer(x, src, dst, et, Wr, Wroot, b):
            N, d = x.shape
            R = Wr.shape[0]
            xW = jnp.einsum('nd,rdh->rnh', x, Wr)
            m = xW[et, src]
            seg = dst * R + et
            counts = jax.ops.segment_sum(jnp.ones((m.shape[0],), dtype=x.dtype), seg, num_segments=N * R)
            norm = 1.0 / jnp.maximum(counts, 1.0)
            m = m * norm[seg][:, None]
            agg = jax.ops.segment_sum(m, dst, num_segments=N)
            return agg + x @ Wroot + b
        src, dst = (edge_index[0], edge_index[1])
        x = node_emb
        n_layers = W.shape[0]
        for i in range(n_layers):
            x = _rgcn_layer(x, src, dst, edge_type, W[i], W_root[i], bias[i])
            if i < n_layers - 1:
                x = jax.nn.relu(x)
        return x

    def _L1_gnn_ref(x, i, j, rbf, Wf1, bf1, Wf2, bf2, Wl, bl, gamma, beta):
        import jax, jax.numpy as jnp
        import numpy as np
        N, E, D, K = (12500, 156250, 64, 64)
        Wxh = x @ Wl.T + bl
        h = jax.nn.silu(rbf @ Wf1.T + bf1)
        f_ij = h @ Wf2.T + bf2
        msg = f_ij * Wxh[j]
        agg = jax.ops.segment_sum(msg, i, num_segments=x.shape[0])
        y = x + agg
        mu = jnp.mean(y, axis=-1, keepdims=True)
        var = jnp.var(y, axis=-1, keepdims=True)
        return (y - mu) * jax.lax.rsqrt(var + 1e-05) * gamma + beta
    edge_index = jnp.stack([src, dst])
    h = jnp.maximum(_layernorm(x, axis=-1), 0.0)
    x = x + _L0_gnn_ref(edge_index, edge_type_16, h, L0_gnn_W, L0_gnn_W_root, L0_gnn_bias)
    h = jnp.maximum(_layernorm(x, axis=-1), 0.0)
    x = x + _L1_gnn_ref(h, src, dst, edge_attr_64, L1_gnn_Wf1, L1_gnn_bf1, L1_gnn_Wf2, L1_gnn_bf2, L1_gnn_Wl, L1_gnn_bl, L1_gnn_gamma, L1_gnn_beta)
    return x

_drawn_inputs = setup_inputs


def setup_inputs(seed=0):
    import zlib

    import numpy as np

    out = dict(_drawn_inputs(seed))
    spreads = {'L0_gnn_bias': (0.0, 0.1), 'L1_gnn_gamma': (1.0, 0.6), 'L1_gnn_beta': (0.0, 0.8)}
    factors = {'edge_attr_64': 8.0, 'L1_gnn_bf1': 5.702, 'L1_gnn_bl': 5.838}
    for name, (base, spread) in spreads.items():
        noise = np.random.default_rng([zlib.crc32(name.encode()), seed]).standard_normal(out[name].shape)
        drawn = base * np.exp(spread * noise) if base else spread * noise
        out[name] = jnp.asarray(drawn.astype(out[name].dtype))
    for name, factor in factors.items():
        out[name] = (out[name] * factor).astype(out[name].dtype)
    return out
```

```python
import concourse.bass as bass
from concourse import mybir
from contextlib import ExitStack

P = 128
N, D, R, E = 12500, 64, 16, 400000
LAYERS = 3
EPS = 1e-5
TILES = -(-N // P)
NP = TILES * P
FULL = N // P
REST = N - FULL * P
C = 5
GE = C * P
NG = E // GE
SLOTS = 5
ITERS = NG // SLOTS
GB = 125
NB = NG // GB
W = 64
ROUNDS = NP // W
BASE_MAX = NP - W
BK = -(-N // P)
NSG = NG + BK
SITER = 3
DM = D + 1
ZR = 64
ZB = GE // ZR
FAR = 100000.0
BANK = 512
assert NSG % SITER == 0 and BK * C <= BANK and BK <= P and P * C >= NG and (BK - 2) % 16 == 0
assert NG * GE == E and ITERS * SLOTS == NG and NB * GB == NG and TILES % 2 == 0

F32, I32, BF16 = mybir.dt.float32, mybir.dt.int32, mybir.dt.bfloat16
ALU = mybir.AluOpType
ACT = mybir.ActivationFunctionType
AX = mybir.AxisListType


def gnn_program(nc, x, src, dst, edge_attr, edge_type, w_rel, w_root, bias,
                wf1, bf1, wf2, bf2, wl, bl, gamma, beta, out):
    table = nc.dram_tensor("rel_table", (NP * R, D), F32, kind="Internal").ap()
    wxh = nc.dram_tensor("wxh_table", (NP, D), F32, kind="Internal").ap()
    dst_main = nc.dram_tensor("dst_main", (P, NG * C), F32, kind="Internal").ap()
    dst_missed = nc.dram_tensor("dst_missed", (P, NG * C), F32, kind="Internal").ap()
    base_main = nc.dram_tensor("base_main", (1, NG), I32, kind="Internal").ap()
    base_missed = nc.dram_tensor("base_missed", (1, NG), I32, kind="Internal").ap()
    dst_idx = nc.dram_tensor("dst_idx", (P, NG * C), I32, kind="Internal").ap()
    bucketed = nc.dram_tensor("bucketed", (NSG * GE, DM), F32, kind="Internal").ap()

    ctx = ExitStack()
    with ctx:
        def sb(name, shape, dt=F32):
            return ctx.enter_context(nc.sbuf_tensor(name, shape, dt))

        def sem(name):
            return ctx.enter_context(nc.semaphore(name))

        wide = sb("wide", [P, NP])
        cnt = wide[0:R, :]
        agg = wide[D:2 * D, :]
        xn = sb("xn", [P, TILES, D])
        x1 = sb("x1", [P, TILES, D])
        scratch = wide[:, 0:TILES * D].rearrange("p (t d) -> p t d", d=D)
        dstloc = sb("dstloc", [P, NG * C])
        idx = sb("idx", [P, NG * C], I32)
        etf = sb("etf", [P, NG * C])
        norm = sb("norm", [P, NG * C])
        base = sb("base", [1, NG], I32)
        base_f = wide[0:1, 3 * NB * GE:3 * NB * GE + NG]
        base_b = wide[0:1, 3 * NB * GE + NG:3 * NB * GE + 2 * NG].bitcast(I32)
        base_s = sb("base_s", [1, NSG], I32)
        miss = sb("miss", [P, 1])
        miss_i = sb("miss_i", [1, 1], I32)
        iota_i = wide[:, 3 * NB * GE + 2 * NG:3 * NB * GE + 2 * NG + P].bitcast(I32)
        iota = sb("iota", [P, P])
        iota_b = sb("iota_b", [P, W], BF16)
        part_i = sb("part_i", [P, 1], I32)
        part = sb("part", [P, 1])
        ident = sb("ident", [P, P])
        ones = sb("ones", [P, P])
        before = sb("before", [P, P])
        ones_b = sb("ones_b", [P, P], BF16)
        before_b = sb("before_b", [P, P], BF16)
        wrel_sb = sb("wrel_sb", [D, R, D])
        wroot_sb = sb("wroot_sb", [D + 1, LAYERS, D])
        wl_t = sb("wl_t", [D + 1, D])
        wf2_t = sb("wf2_t", [D + 1, D])
        wf1_t = sb("wf1_t", [D, D])
        wraw = sb("wraw", [D, 3, D])
        bf1_sb = sb("bf1_sb", [D, 1])
        gamma_sb = sb("gamma_sb", [P, D])
        beta_sb = sb("beta_sb", [P, D])
        mean = sb("mean", [P, TILES])
        var = sb("var", [P, TILES])
        rstd = sb("rstd", [P, TILES])
        idx_ring = sb("idx_ring", [P, SLOTS, C], I32)
        rows = sb("rows", [P, SLOTS, C, D])
        ring = sb("ring", [P, SLOTS * C * (W + DM)])
        onehot = ring[:, 0:SLOTS * C * W].rearrange("p (s c w) -> p s c w", s=SLOTS, c=C)
        onehot_w = ring[:, SLOTS * C * W:2 * SLOTS * C * W].rearrange("p (s c w) -> p s c w", s=SLOTS, c=C)
        msgs = ring[:, SLOTS * C * W:SLOTS * C * (W + DM)].rearrange("p (s c f) -> p s c f", s=SLOTS, c=C)
        onehot_s = ring[:, 0:SITER * C * P].rearrange("p (s c n) -> p s c n", s=SITER, c=C)
        onehot_b = onehot[:, :, :, :].rearrange("p s c w -> p s (c w)").bitcast(BF16)
        types = sb("types", [P, SLOTS, C, R])
        types_b = sb("types_b", [P, SLOTS, C, R], BF16)
        norm_add = sb("norm_add", [P, C])
        attr_ring = sb("attr_ring", [P, SLOTS * C * D])
        attr = attr_ring[:, :].rearrange("p (s c d) -> p s c d", s=SLOTS, c=C)
        sorted_in = attr_ring[:, 0:SITER * C * DM].rearrange("p (s c f) -> p s c f", s=SITER, c=C)
        attr_t = sb("attr_t", [D, GE])
        types_t = attr_t[0:R, :].rearrange("r (c p) -> r c p", c=C)
        onehot_t = sb("onehot_t", [D, GE])
        window_in = sb("window_in", [D, SLOTS, D])
        slot_ring = sb("slot_ring", [P, SLOTS, C], I32)
        hi_i = sb("hi_i", [P, C], I32)
        lo_i = sb("lo_i", [P, SLOTS, C], I32)
        bucket_b = sb("bucket_b", [P, C, BK], BF16)
        place = sb("place", [P, C, BK])
        filled = sb("filled", [P, BK])
        slot_f = sb("slot_f", [P, C])
        zero_idx = sb("zero_idx", [BK, ZB], I32)
        hid_t = sb("hid_t", [D + 1, GE])
        rows_in = sb("rows_in", [P, 2, D])
        feat = sb("feat", [D + 1, 2, P])
        rel_out = ring[:, 0:2 * R * D].rearrange("p (k f) -> p k f", k=2)

        ps = ctx.enter_context(nc.psum_tensor("ps", [P, 8 * BANK], F32))

        def bank(b, width=BANK):
            return ps[:, b * BANK:b * BANK + width]

        dve_step = sem("dve_step")
        loaded = sem("loaded")
        stored = sem("stored")
        iota_done = sem("iota_done")
        pass_sems = []

        def psem(name):
            s = sem(name)
            pass_sems.append(s)
            return s

        gathered = [psem(f"gathered{s}") for s in range(SLOTS)]
        idx_ready = [psem(f"idx_ready{s}") for s in range(SLOTS)]
        attr_ready = [psem(f"attr_ready{s}") for s in range(SLOTS)]
        pool_go = psem("pool_go")
        pe_go = psem("pe_go")
        onehot_made = psem("onehot_made")
        weights_ready = psem("weights_ready")
        types_ready = psem("types_ready")
        types_turned = psem("types_turned")
        types_t_ready = psem("types_t_ready")
        norms_ready = psem("norms_ready")
        sum_ready = psem("sum_ready")
        sum_taken = psem("sum_taken")
        attr_turned = psem("attr_turned")
        attr_t_ready = psem("attr_t_ready")
        hid_ready = psem("hid_ready")
        hid_t_ready = psem("hid_t_ready")
        filt_ready = psem("filt_ready")
        msg_ready = psem("msg_ready")
        norm_red = psem("norm_red")
        scattered = [psem(f"scattered{s}") for s in range(SLOTS)]
        slots_ready = [psem(f"slots_ready{s}") for s in range(SLOTS)]
        window_ready = [psem(f"window_ready{s}") for s in range(SLOTS)]
        sorted_ready = [psem(f"sorted_ready{s}") for s in range(SITER)]
        zeroed = psem("zeroed")
        static_zeroed = psem("static_zeroed")
        hi_made = psem("hi_made")
        bucket_ready = psem("bucket_ready")
        bucket_sums = psem("bucket_sums")
        place_step = psem("place_step")
        filled_done = psem("filled_done")
        onehot_turned = psem("onehot_turned")
        onehot_t_ready = psem("onehot_t_ready")
        wrows_made = psem("wrows_made")
        wrows_ready = psem("wrows_ready")
        lo_made = psem("lo_made")
        tile_in = psem("tile_in")
        tile_turned = psem("tile_turned")
        tile_feat = psem("tile_feat")
        tile_prod = psem("tile_prod")
        tile_root = psem("tile_root")
        evac_v = psem("evac_v")
        evac_s = psem("evac_s")
        agg_set = psem("agg_set")
        tile_stored = [psem(f"tile_stored{k}") for k in range(2)]
        sem_nums = [s.num for s in pass_sems]
        assert sem_nums == list(range(sem_nums[0], sem_nums[0] + len(sem_nums)))

        def clear_pass_sems():
            with nc.Block() as block:
                @block.gpsimd
                def _(pool):
                    pool.dma_reset(range(sem_nums[0], sem_nums[-1] + 1))
                    pool.sem_clear(range(sem_nums[0], sem_nums[-1] + 1))

        steps = [0]

        def link(dve, ins):
            steps[0] += 1
            ins.then_inc(dve_step, 1)
            dve.wait_ge(dve_step, steps[0])

        loads = [0]

        def load(eng, to, frm):
            loads[0] += 16
            eng.dma_start(to, frm).then_inc(loaded, 16)

        stores = [0]

        raw = wide[0:GB, 0:3 * NB * GE].bitcast(I32).rearrange("q (k b e) -> q k b e", k=3, b=NB)
        dst_rows = xn[0:GB, :, :].rearrange("q t d -> q (t d)")[:, 0:NB * GE]
        idx_rows = x1[0:GB, :, :].rearrange("q t d -> q (t d)")[:, 0:NB * GE]

        with nc.Block() as block:
            @block.sync
            def _(sp):
                for k, a in enumerate((dst, src, edge_type)):
                    load(sp, raw[:, k], a.rearrange("(b q e) -> q b e", b=NB, q=GB))
                with nc.allow_non_contiguous_dma(reason="first destination of each group"):
                    load(sp, base[:, :], dst.rearrange("(o g e) -> o g e", o=1, e=GE)[:, :, 0])
                load(sp, wroot_sb[0:D, :, :], w_root.rearrange("l i o -> i l o"))
                load(sp, wroot_sb[D:D + 1, :, :], bias.rearrange("(a l) o -> a l o", a=1))
                for k, a in enumerate((wl, wf1, wf2)):
                    load(sp, wraw[:, k, :], a)
                load(sp, wl_t[D:D + 1, :], bl.rearrange("(a d) -> a d", a=1))
                load(sp, wf2_t[D:D + 1, :], bf2.rearrange("(a d) -> a d", a=1))
                load(sp, bf1_sb[:, :], bf1.rearrange("(d a) -> d a", a=1))
                load(sp, gamma_sb[:, :], gamma.rearrange("(a d) -> a d", a=1).to_broadcast([P, D]))
                load(sp, beta_sb[:, :], beta.rearrange("(a d) -> a d", a=1).to_broadcast([P, D]))
                sp.wait_ge(loaded, loads[0])

            @block.gpsimd
            def _(pool):
                nc.gpsimd.iota(iota_i[:, :], pattern=[[1, P]], base=0, channel_multiplier=0).then_inc(iota_done, 1)
                nc.gpsimd.iota(part_i[:, :], pattern=[[0, 1]], base=0, channel_multiplier=1).then_inc(iota_done, 1)

            @block.vector
            def _(dve):
                nc.vector.memset(ones[:, :], 1.0)
                nc.vector.memset(feat[D:D + 1, :, :], 1.0)
                nc.vector.memset(hid_t[D:D + 1, :], 1.0)
                dve.wait_ge(iota_done, 2)
                nc.vector.tensor_copy(iota_b[:, :], iota_i[:, 0:W])
                nc.vector.tensor_copy(iota[:, :], iota_i[:, :])
                link(dve, nc.vector.tensor_copy(part[:, :], part_i[:, :]))
                nc.vector.tensor_scalar(ident[:, :], iota[:, :], part[:, 0:1], None, ALU.is_equal)
                nc.vector.tensor_scalar(before[:, :], iota[:, :], part[:, 0:1], None, ALU.is_gt)
                nc.vector.tensor_scalar(before_b[:, :], iota[:, :], part[:, 0:1], None, ALU.is_gt)
                nc.vector.memset(ones_b[:, :], 1.0)

        with nc.Block() as block:
            @block.vector
            def _(dve):
                nc.vector.tensor_copy(dst_rows, raw[:, 0].rearrange("q b e -> q (b e)"))
                nc.vector.tensor_scalar(base[:, :], base[:, :], float(BASE_MAX), None, ALU.min).then_inc(dve_step, 1)
                steps[0] += 1
                link(dve, nc.vector.tensor_scalar(idx_rows, raw[:, 1].rearrange("q b e -> q (b e)"),
                                                  float(R), None, ALU.mult))
                nc.vector.tensor_tensor(idx_rows, idx_rows, raw[:, 2].rearrange("q b e -> q (b e)"), ALU.add)
                nc.vector.tensor_copy(base_f[:, :], base[:, :])
                nc.vector.memset(base_b[:, :], -W)

        turned = sem("turned")
        untangled = sem("untangled")
        with nc.Block() as block:
            @block.tensor
            def _(pe):
                nc.tensor.matmul(bank(7), ones[0:1, :], base_f[:, 0:BANK], start=True, stop=True)
                nc.tensor.matmul(bank(6, NG - BANK), ones[0:1, :], base_f[:, BANK:NG], start=True, stop=True)
                for k, w in enumerate((wl_t, wf1_t, wf2_t)):
                    ins = nc.tensor.transpose(ps[0:D, 5 * BANK + k * D:5 * BANK + (k + 1) * D], wraw[:, k, :],
                                              ident[0:D, 0:D])
                ins.then_inc(turned, 1)
                n = 0
                for rows_f in (dst_rows, idx_rows):
                    v = rows_f.rearrange("q (b p c) -> q b p c", b=NB, c=C)
                    for b in range(NB):
                        for c in range(C):
                            if n >= 4:
                                pe.wait_ge(untangled, 1 + n - 3)
                            nc.tensor.transpose(bank(n % 4, GB), v[:, b, :, c], ident[0:GB, 0:GB]).then_inc(turned, 1)
                            n += 1

            @block.vector
            def _(dve):
                dve.wait_ge(turned, 1)
                for k, w in enumerate((wl_t, wf1_t, wf2_t)):
                    ins = nc.vector.tensor_copy(w[0:D, :], ps[0:D, 5 * BANK + k * D:5 * BANK + (k + 1) * D])
                ins.then_inc(untangled, 1)
                n = 0
                for to in (norm, idx):
                    v = to[:, :].rearrange("p (b g c) -> p b g c", b=NB, c=C)
                    for b in range(NB):
                        for c in range(C):
                            dve.wait_ge(turned, n + 2)
                            nc.vector.tensor_copy(v[:, b, :, c], bank(n % 4, GB)).then_inc(untangled, 1)
                            n += 1
                dve.wait_ge(untangled, n + 1)
                dv = norm[:, :].rearrange("p (g c) -> p g c", c=C)
                lv = dstloc[:, :].rearrange("p (g c) -> p g c", c=C)
                nc.vector.tensor_tensor(lv[:, 0:BANK, :], dv[:, 0:BANK, :],
                                        bank(7).unsqueeze(2).to_broadcast([P, BANK, C]), ALU.subtract)
                link(dve, nc.vector.tensor_tensor(lv[:, BANK:NG, :], dv[:, BANK:NG, :],
                                                  bank(6, NG - BANK).unsqueeze(2).to_broadcast([P, NG - BANK, C]),
                                                  ALU.subtract))
                sc = wide[:, 0:NG * C]
                dst_i = wide[:, 2 * NG * C:3 * NG * C].bitcast(I32)
                sd = wide[:, NG * C:2 * NG * C]
                link(dve, nc.vector.tensor_scalar(sc, dstloc[:, :], 0.0, None, ALU.is_ge))
                link(dve, nc.vector.tensor_scalar(sd, dstloc[:, :], float(W), None, ALU.is_lt))
                link(dve, nc.vector.tensor_tensor(sc, sc, sd, ALU.mult))
                link(dve, nc.vector.tensor_reduce(miss[:, :], sc, axis=AX.X, op=ALU.add))
                nc.vector.tensor_copy(dst_i, norm[:, :])
                link(dve, nc.vector.tensor_scalar(sc, sc, -FAR, float(W), ALU.mult, ALU.add))
                link(dve, nc.vector.tensor_tensor(norm[:, :], norm[:, :], sc, ALU.add))
                sdi = sd.bitcast(I32)
                link(dve, nc.vector.tensor_scalar(sdi, idx[:, :], R - 1, None, ALU.bitwise_and))
                nc.vector.tensor_copy(etf[:, :], sdi)
                link(dve, nc.vector.tensor_scalar(miss[:, :], miss[:, :], -1.0, float(NG * C), ALU.mult, ALU.add))

        missed = sem("missed")
        with nc.Block() as block:
            @block.tensor
            def _(pe):
                nc.tensor.matmul(ps[0:1, 0:1], miss[:, :], ones[:, 0:1], start=True, stop=True).then_inc(missed, 1)

            @block.vector
            def _(dve):
                dve.wait_ge(missed, 1)
                nc.vector.tensor_copy(miss_i[:, :], ps[0:1, 0:1])

            @block.sync
            def _(sp):
                sp.dma_start(dst_main, dstloc[:, :]).then_inc(stored, 16)
                sp.dma_start(dst_missed, norm[:, :]).then_inc(stored, 16)
                sp.dma_start(base_main, base[:, :]).then_inc(stored, 16)
                sp.dma_start(dst_idx, wide[:, 2 * NG * C:3 * NG * C].bitcast(I32)).then_inc(stored, 16)
                sp.dma_start(base_missed, base_b[:, :]).then_inc(stored, 16)
                sp.wait_ge(stored, 80)

        def make_onehot(i, s, dtype_b):
            loc = dstloc[:, bass.ds(i * (SLOTS * C) + s * C, C)].unsqueeze(2).to_broadcast([P, C, W])
            if dtype_b:
                to = onehot_b[:, s, 0:C * W].rearrange("p (c w) -> p c w", w=W)
                return nc.vector.tensor_tensor(to, iota_b[:, :].unsqueeze(1).to_broadcast([P, C, W]), loc, ALU.is_equal)
            return nc.vector.tensor_tensor(onehot[:, s], iota[:, 0:W].unsqueeze(1).to_broadcast([P, C, W]), loc,
                                           ALU.is_equal)

        def make_types(i, s, to):
            et = etf[:, bass.ds(i * (SLOTS * C) + s * C, C)].unsqueeze(2).to_broadcast([P, C, R])
            return nc.vector.tensor_tensor(to[:, s], iota[:, 0:R].unsqueeze(1).to_broadcast([P, C, R]), et,
                                           ALU.is_equal)

        def window(eng, i, s):
            return eng.value_load(base[0:1, bass.ds(i * SLOTS + s, 1)], min_val=0, max_val=BASE_MAX)

        def count_pass():
            with nc.Block() as block:
                @block.vector
                def _(dve):
                    def operands(i, s):
                        make_onehot(i, s, True)
                        make_types(i, s, types_b).then_inc(types_ready, 1)

                    def body(i, last):
                        for s in range(SLOTS):
                            if s + 1 < SLOTS:
                                operands(i, s + 1)
                            elif not last:
                                operands(i + 1, 0)
                            n = i * SLOTS + s
                            at = cnt[:, bass.ds(window(dve, i, s), W)]
                            dve.wait_ge(sum_ready, n + 1)
                            dve.wait_ge(sum_taken, n + 2)
                            nc.vector.tensor_tensor(at, at, ps[0:R, s * BANK:s * BANK + W], ALU.add).then_inc(sum_taken, 1)

                    dve.sem_inc(sum_taken, 2)
                    operands(0, 0)
                    with dve.Fori(0, ITERS - 1) as i:
                        body(i, False)
                    body(ITERS - 1, True)
                    dve.wait_ge(sum_taken, NG + 2)

                @block.tensor
                def _(pe):
                    with pe.Fori(0, ITERS) as i:
                        for s in range(SLOTS):
                            pe.wait_ge(types_ready, i * SLOTS + s + 1)
                            for c in range(C):
                                ins = nc.tensor.matmul(ps[0:R, s * BANK:s * BANK + W], types_b[:, s, c, :],
                                                       onehot_b[:, s, c * W:(c + 1) * W],
                                                       start=(c == 0), stop=(c == C - 1))
                            ins.then_inc(sum_ready, 1)
            clear_pass_sems()

        zeros = x1[:, :, :].rearrange("p t d -> p (t d)")[:, 0:ZR * DM]
        blocks = bucketed.rearrange("(b r) f -> b (r f)", r=ZR)

        def gather_rows(block, frm, zero_first=False):
            @block.gpsimd
            def _(pool):
                if zero_first:
                    pool.wait_ge(static_zeroed, 16 * ZB + 16)
                    for j in range(ZB):
                        nc.gpsimd.indirect_dma_start(
                            out=blocks, out_offset=bass.IndirectOffsetOnAxis(ap=zero_idx[:, j:j + 1], axis=0),
                            in_=zeros[0:BK, :], in_offset=None).then_inc(zeroed, 16)
                    pool.wait_ge(zeroed, 16 * ZB)
                with pool.Fori(0, ITERS) as i:
                    for s in range(SLOTS):
                        pool.wait_ge(idx_ready[s], i * 16 + 16)
                        nc.gpsimd.sem_inc(pool_go, 1)
                        for c in range(C):
                            nc.gpsimd.indirect_dma_start(
                                out=rows[:, s, c, :], out_offset=None, in_=frm,
                                in_offset=bass.IndirectOffsetOnAxis(ap=idx_ring[:, s, c:c + 1], axis=0),
                            ).then_inc(gathered[s], 16)

        def chunk_cols(i, s):
            return bass.ds(i * (SLOTS * C) + s * C, C)

        def feed_idx(sp, i, s):
            sp.wait_ge(sum_taken, i * SLOTS + s + 1)
            sp.dma_start(idx_ring[:, s, :], idx[:, chunk_cols(i, s)]).then_inc(idx_ready[s], 16)

        def make_buckets(dve, i, s):
            n = i * SLOTS + s
            nc.vector.tensor_scalar(hi_i[:, :], idx[:, chunk_cols(i, s)], 11, None,
                                    ALU.logical_shift_right).then_inc(hi_made, 1)
            dve.wait_ge(hi_made, n + 1)
            nc.vector.tensor_tensor(bucket_b[:, :, :], iota[:, 0:BK].unsqueeze(1).to_broadcast([P, C, BK]),
                                    hi_i[:, :].unsqueeze(2).to_broadcast([P, C, BK]),
                                    ALU.is_equal).then_inc(bucket_ready, 1)

        def add_sum(dve, i, s, at):
            n = i * SLOTS + s
            dve.wait_ge(sum_ready, n + 1)
            dve.wait_ge(sum_taken, n + SLOTS)
            nc.vector.tensor_tensor(at, at, ps[0:D, 0:W], ALU.add).then_inc(sum_taken, 1)

        def layer_pass(layer, first_round):
            first_layer = layer == 0
            count = layer == 1 and first_round
            rank = layer == 2 and first_round
            with nc.Block() as block:
                @block.sync
                def _(sp):
                    if rank:
                        for j in range(ZB):
                            sp.dma_start(blocks[(NG + 1) * ZB:(NSG - 1) * ZB, :].rearrange(
                                "(g j) x -> j g x", j=ZB)[j], zeros[0:BK - 2, :]).then_inc(static_zeroed, 16)
                        sp.dma_start(blocks[(NSG - 1) * ZB:NSG * ZB, :], zeros[0:ZB, :]).then_inc(static_zeroed, 16)
                    with sp.Fori(0, ITERS) as i:
                        for s in range(SLOTS):
                            feed_idx(sp, i, s)

                gather_rows(block, table, zero_first=rank)

                @block.scalar
                def _(act):
                    if first_layer:
                        with act.Fori(0, ITERS) as i:
                            for s in range(SLOTS):
                                act.wait_ge(types_turned, i * SLOTS + s + 1)
                                nc.scalar.copy(types_t[:, :, :].rearrange("r c p -> r (c p)"),
                                               ps[0:R, 2 * BANK:2 * BANK + GE]).then_inc(types_t_ready, 1)

                @block.vector
                def _(dve):
                    dve.sem_inc(sum_taken, SLOTS)
                    dve.sem_inc(filled_done, 1)
                    with dve.Fori(0, ITERS) as i:
                        for s in range(SLOTS):
                            n = i * SLOTS + s
                            cols = bass.ds(i * (SLOTS * C) + s * C, C)
                            if first_layer:
                                make_types(i, s, types).then_inc(types_ready, 1)
                            if count or rank:
                                make_buckets(dve, i, s)
                            make_onehot(i, s, False).then_inc(onehot_made, 1)
                            if first_layer:
                                dve.wait_ge(norms_ready, n + 1)
                                wt = ps[:, BANK:BANK + C * W].rearrange("p (c w) -> p c w", w=W)
                            else:
                                wt = norm[:, cols].unsqueeze(2).to_broadcast([P, C, W])
                            dve.wait_ge(onehot_made, n + 1)
                            nc.vector.tensor_tensor(onehot_w[:, s], onehot[:, s], wt, ALU.mult).then_inc(weights_ready, 1)
                            if first_layer:
                                dve.wait_ge(weights_ready, n + 1)
                                if first_round:
                                    nc.vector.tensor_reduce(norm[:, cols], onehot_w[:, s], axis=AX.X, op=ALU.add)
                                else:
                                    nc.vector.tensor_reduce(norm_add[:, :], onehot_w[:, s], axis=AX.X,
                                                            op=ALU.add).then_inc(norm_red, 1)
                                    dve.wait_ge(norm_red, n + 1)
                                    nc.vector.tensor_tensor(norm[:, cols], norm[:, cols], norm_add[:, :], ALU.add)
                            if count or rank:
                                dve.wait_ge(bucket_sums, n + 1)
                            if rank:
                                dve.wait_ge(filled_done, n + 1)
                                nc.vector.tensor_tensor(place[:, :, :], bank(6, C * BK).rearrange(
                                    "p (c b) -> p c b", c=C), filled[:, :].unsqueeze(1).to_broadcast([P, C, BK]),
                                    ALU.add).then_inc(place_step, 1)
                                dve.wait_ge(place_step, 3 * n + 1)
                                nc.vector.tensor_tensor(place[:, :, :], place[:, :, :], bucket_b[:, :, :],
                                                        ALU.mult).then_inc(place_step, 1)
                                dve.wait_ge(place_step, 3 * n + 2)
                                nc.vector.tensor_reduce(slot_f[:, :], place[:, :, :], axis=AX.X,
                                                        op=ALU.add).then_inc(place_step, 1)
                                dve.wait_ge(place_step, 3 * n + 3)
                                nc.vector.tensor_copy(etf[:, cols].bitcast(I32), slot_f[:, :])
                            if count or rank:
                                dve.wait_ge(filled_done, n + 1)
                                nc.vector.tensor_tensor(filled[:, :], filled[:, :], bank(7, BK),
                                                        ALU.add).then_inc(filled_done, 1)
                            add_sum(dve, i, s, agg[:, bass.ds(window(dve, i, s), W)])
                    dve.wait_ge(sum_taken, NG + SLOTS)

                @block.tensor
                def _(pe):
                    with pe.Fori(0, ITERS) as i:
                        for s in range(SLOTS):
                            n = i * SLOTS + s
                            if count or rank:
                                pe.wait_ge(bucket_ready, n + 1)
                                pe.wait_ge(filled_done, n + 1)
                                if rank:
                                    nc.tensor.matmul(bank(6, C * BK), before_b[:, :], bucket_b[:, :, :].rearrange(
                                        "p c b -> p (c b)"), start=True, stop=False)
                                    for c in range(C - 1):
                                        nc.tensor.matmul(bank(6, C * BK)[:, (c + 1) * BK:C * BK].rearrange(
                                            "p (c b) -> p c b", b=BK), ones_b[:, :], bucket_b[:, c:c + 1, :].to_broadcast(
                                            [P, C - 1 - c, BK]), start=False, stop=(c == C - 2))
                                for c in range(C):
                                    ins = nc.tensor.matmul(bank(7, BK), ones_b[:, :], bucket_b[:, c, :],
                                                           start=(c == 0), stop=(c == C - 1))
                                ins.then_inc(bucket_sums, 1)
                            if first_layer:
                                pe.wait_ge(types_ready, n + 1)
                                for c in range(C):
                                    ins = nc.tensor.transpose(ps[0:R, 2 * BANK + c * P:2 * BANK + (c + 1) * P],
                                                              types[:, s, c, :], ident[:, :])
                                ins.then_inc(types_turned, 1)
                                at = cnt[:, bass.ds(window(pe, i, s), W)]
                                pe.wait_ge(types_t_ready, n + 1)
                                for c in range(C):
                                    ins = nc.tensor.matmul(ps[:, BANK + c * W:BANK + (c + 1) * W], types_t[:, c, :], at,
                                                           start=True, stop=True)
                                ins.then_inc(norms_ready, 1)
                            pe.wait_ge(weights_ready, n + 1)
                            pe.wait_ge(gathered[s], i * (16 * C) + 16 * C)
                            pe.wait_ge(sum_taken, n + SLOTS)
                            for c in range(C):
                                ins = nc.tensor.matmul(ps[0:D, 0:W], rows[:, s, c, :], onehot_w[:, s, c, :],
                                                       start=(c == 0), stop=(c == C - 1))
                            ins.then_inc(sum_ready, 1)
            clear_pass_sems()

        def message_pass(windowed):
            with nc.Block() as block:
                @block.sync
                def _(sp):
                    av = edge_attr.rearrange("(g p c) d -> g p (c d)", p=P, c=C)

                    def body(i, first):
                        for s in range(SLOTS):
                            n = i * SLOTS + s
                            if windowed:
                                row = window(sp, i, s)
                            if not first:
                                sp.wait_ge(scattered[s], i * (16 * C))
                            sp.dma_start(attr[:, s, :, :].rearrange("p c d -> p (c d)"),
                                         av[bass.ds(n, 1), :, :].rearrange("o p f -> p (o f)")
                                         ).then_inc(attr_ready[s], 16)
                            if windowed:
                                sp.dma_start(window_in[:, s, :], wxh[bass.ds(row, W), :]).then_inc(window_ready[s], 16)
                            else:
                                sp.dma_start(idx_ring[:, s, :], dst_idx[:, chunk_cols(i, s)]).then_inc(idx_ready[s], 16)
                            sp.dma_start(slot_ring[:, s, :], etf[:, chunk_cols(i, s)].bitcast(I32)
                                         ).then_inc(slots_ready[s], 16)

                    body(0, True)
                    with sp.Fori(1, ITERS) as i:
                        body(i, False)
                    for s in range(SLOTS):
                        sp.wait_ge(scattered[s], ITERS * 16 * C)

                @block.gpsimd
                def _(pool):
                    def gather(i, s):
                        pool.wait_ge(idx_ready[s], i * 16 + 16)
                        nc.gpsimd.sem_inc(pool_go, 1)
                        for c in range(C):
                            nc.gpsimd.indirect_dma_start(
                                out=rows[:, s, c, :], out_offset=None, in_=wxh,
                                in_offset=bass.IndirectOffsetOnAxis(ap=idx_ring[:, s, c:c + 1], axis=0),
                            ).then_inc(gathered[s], 16)

                    with pool.Fori(0, ITERS) as i:
                        if not windowed:
                            for s in range(SLOTS):
                                gather(i, s)
                        for s in range(SLOTS):
                            pool.wait_ge(slots_ready[s], i * 16 + 16)
                            pool.wait_ge(msg_ready, i * SLOTS + s + 2)
                            nc.gpsimd.sem_inc(pool_go, 1)
                            for c in range(C):
                                nc.gpsimd.indirect_dma_start(
                                    out=bucketed, in_=msgs[:, s, c, :], in_offset=None,
                                    out_offset=bass.IndirectOffsetOnAxis(ap=slot_ring[:, s, c:c + 1], axis=0),
                                ).then_inc(scattered[s], 16)

                @block.tensor
                def _(pe):
                    def turn(i, s):
                        pe.wait_ge(attr_ready[s], i * 16 + 16)
                        nc.tensor.sem_inc(pe_go, 1)
                        for c in range(C):
                            ins = nc.tensor.transpose(ps[0:D, 2 * BANK + c * P:2 * BANK + (c + 1) * P],
                                                      attr[:, s, c, :], ident[:, :])
                        ins.then_inc(attr_turned, 1)

                    def turn_onehot(i, s):
                        if windowed:
                            pe.wait_ge(onehot_made, i * SLOTS + s + 1)
                            nc.tensor.sem_inc(pe_go, 1)
                            for c in range(C):
                                ins = nc.tensor.transpose(ps[0:W, 6 * BANK + c * P:6 * BANK + (c + 1) * P],
                                                          onehot[:, s, c, :], ident[:, :])
                            ins.then_inc(onehot_turned, 1)

                    def hidden(i, s):
                        pe.wait_ge(attr_t_ready, i * SLOTS + s + 1)
                        nc.tensor.sem_inc(pe_go, 1)
                        nc.tensor.matmul(ps[0:D, 4 * BANK:5 * BANK], wf1_t[:, :], attr_t[:, 0:BANK],
                                         start=True, stop=True)
                        nc.tensor.matmul(ps[0:D, 5 * BANK:4 * BANK + GE], wf1_t[:, :], attr_t[:, BANK:GE],
                                         start=True, stop=True).then_inc(hid_ready, 1)

                    def spread_window(i, s):
                        if windowed:
                            pe.wait_ge(onehot_t_ready, i * SLOTS + s + 1)
                            pe.wait_ge(window_ready[s], i * 16 + 16)
                            pe.wait_ge(wrows_ready, i * SLOTS + s + 1)
                            for c in range(C):
                                ins = nc.tensor.matmul(ps[:, c * D:(c + 1) * D], onehot_t[:, c * P:(c + 1) * P],
                                                       window_in[:, s, :], start=True, stop=True)
                            ins.then_inc(wrows_made, 1)

                    def filt(i, s):
                        pe.wait_ge(hid_t_ready, i * SLOTS + s + 1)
                        pe.wait_ge(msg_ready, i * SLOTS + s + 1)
                        for c in range(C):
                            ins = nc.tensor.matmul(ps[:, BANK + c * D:BANK + (c + 1) * D], hid_t[:, c * P:(c + 1) * P],
                                                   wf2_t[:, :], start=True, stop=True)
                        ins.then_inc(filt_ready, 1)

                    def body(i, last):
                        for s in range(SLOTS):
                            hidden(i, s)
                            spread_window(i, s)
                            if s + 1 < SLOTS:
                                turn(i, s + 1)
                                turn_onehot(i, s + 1)
                            elif not last:
                                turn(i + 1, 0)
                                turn_onehot(i + 1, 0)
                            filt(i, s)

                    turn(0, 0)
                    turn_onehot(0, 0)
                    with pe.Fori(0, ITERS - 1) as i:
                        body(i, False)
                    body(ITERS - 1, True)

                @block.scalar
                def _(act):
                    act.sem_inc(wrows_ready, 1)
                    with act.Fori(0, ITERS) as i:
                        for s in range(SLOTS):
                            n = i * SLOTS + s
                            act.wait_ge(attr_turned, n + 1)
                            nc.scalar.copy(attr_t[:, :], ps[0:D, 2 * BANK:2 * BANK + GE]).then_inc(attr_t_ready, 1)
                            if windowed:
                                act.wait_ge(onehot_turned, n + 1)
                                nc.scalar.copy(onehot_t[:, :], ps[0:W, 6 * BANK:6 * BANK + GE]
                                               ).then_inc(onehot_t_ready, 1)
                            act.wait_ge(hid_ready, n + 1)
                            nc.scalar.activation(hid_t[0:D, :], ps[0:D, 4 * BANK:4 * BANK + GE], ACT.Silu,
                                                 bias=bf1_sb[:, 0:1]).then_inc(hid_t_ready, 1)
                            if windowed:
                                act.wait_ge(wrows_made, n + 1)
                                nc.scalar.copy(rows[:, s].rearrange("p c d -> p (c d)"), ps[:, 0:C * D]
                                               ).then_inc(wrows_ready, 1)

                @block.vector
                def _(dve):
                    def window_onehot(i, s):
                        if windowed:
                            make_onehot(i, s, False).then_inc(onehot_made, 1)

                    def body(i, first, last):
                        for s in range(SLOTS):
                            n = i * SLOTS + s
                            if s + 1 < SLOTS:
                                window_onehot(i, s + 1)
                            elif not last:
                                window_onehot(i + 1, 0)
                            nc.vector.tensor_scalar(lo_i[:, s, :], idx[:, chunk_cols(i, s)], 4, P - 1,
                                                    ALU.logical_shift_right, ALU.bitwise_and).then_inc(lo_made, 1)
                            if not first:
                                dve.wait_ge(scattered[s], i * (16 * C))
                            dve.wait_ge(lo_made, n + 1)
                            nc.vector.tensor_copy(msgs[:, s, :, D], lo_i[:, s, :])
                            dve.wait_ge(filt_ready, n + 1)
                            if windowed:
                                dve.wait_ge(wrows_ready, n + 2)
                            else:
                                dve.wait_ge(gathered[s], i * (16 * C) + 16 * C)
                            nc.vector.tensor_tensor(msgs[:, s, :, 0:D], ps[:, BANK:BANK + C * D].rearrange(
                                "p (c d) -> p c d", c=C), rows[:, s], ALU.mult).then_inc(msg_ready, 1)

                    dve.sem_inc(msg_ready, 1)
                    window_onehot(0, 0)
                    body(0, True, False)
                    with dve.Fori(1, ITERS - 1) as i:
                        body(i, False, False)
                    body(ITERS - 1, False, True)
            clear_pass_sems()

        def bucket_plan():
            flat = x1[:, :, :].rearrange("p t d -> p (t d)")
            thr = flat[:, 0:C]
            reach = flat[:, C:C + C * BK].rearrange("p (c b) -> p c b", c=C)
            at = C + C * BK
            whole = flat[:, at:at + BK]
            floor_c = flat[0:BK, at + BK:at + BK + 1]
            groups_c = flat[0:BK, at + BK + 1:at + BK + 2]
            last_c = flat[0:BK, at + BK + 2:at + BK + 3]
            groups_w = flat[0:BK, at + 2 * BK:at + 2 * BK + P]
            at += 2 * BK + P
            part_thr = flat[:, at:at + 1]
            at += 1
            giota_i = flat[0:BK, at:at + NSG].bitcast(I32)
            giota = flat[0:BK, at + NSG:at + 2 * NSG]
            begun = flat[0:BK, at + 2 * NSG:at + 3 * NSG]
            planned = sem("planned")
            with nc.Block() as block:
                @block.gpsimd
                def _(pool):
                    nc.gpsimd.iota(giota_i, pattern=[[1, NSG]], base=0, channel_multiplier=0).then_inc(iota_done, 1)

                @block.vector
                def _(dve):
                    link(dve, nc.vector.tensor_scalar(thr, iota[:, 0:C], float(GE), float(GE), ALU.mult, ALU.add))
                    link(dve, nc.vector.tensor_scalar(part_thr, part[:, :], float(GE * C), None,
                                                      ALU.mult))
                    link(dve, nc.vector.tensor_scalar(thr, thr, part_thr, None, ALU.add))
                    link(dve, nc.vector.tensor_tensor(reach, filled[:, :].unsqueeze(1).to_broadcast([P, C, BK]),
                                                      thr.unsqueeze(2).to_broadcast([P, C, BK]), ALU.is_ge))
                    link(dve, nc.vector.tensor_reduce(whole, reach.rearrange("p c b -> p b c"), axis=AX.X, op=ALU.add))
                    dve.sem_inc(planned, 1)
                    dve.wait_ge(planned, 2)
                    link(dve, nc.vector.tensor_copy(floor_c, ps[0:BK, 0:1]))
                    link(dve, nc.vector.tensor_scalar(groups_c, floor_c, 1.0, None, ALU.add))
                    link(dve, nc.vector.tensor_copy(groups_w, groups_c.to_broadcast([BK, P])))
                    dve.sem_inc(planned, 1)
                    dve.wait_ge(planned, 4)
                    nc.vector.tensor_scalar(filled[:, :], ps[:, BANK:BANK + BK], float(GE), None, ALU.mult)
                    link(dve, nc.vector.tensor_tensor(last_c, floor_c, ps[0:BK, 2 * BANK:2 * BANK + 1], ALU.add))
                    link(dve, nc.vector.tensor_scalar(last_c, last_c, float(ZB), None, ALU.mult))
                    nc.vector.tensor_scalar(zero_idx[:, :], iota[0:BK, 0:ZB], last_c, None, ALU.add)
                    dve.wait_ge(iota_done, 3)
                    link(dve, nc.vector.tensor_copy(giota, giota_i))
                    link(dve, nc.vector.tensor_scalar(begun, giota, ps[0:BK, 2 * BANK:2 * BANK + 1], None, ALU.is_ge))
                    dve.sem_inc(planned, 1)
                    dve.wait_ge(planned, 6)
                    nc.vector.tensor_scalar(base_s[:, :], ps[0:1, 3 * BANK:3 * BANK + NSG], float(P), -float(P),
                                            ALU.mult, ALU.add)
                    dve.wait_ge(dve_step, steps[0])
                    link(dve, nc.vector.memset(flat, 0.0))

                @block.tensor
                def _(pe):
                    pe.wait_ge(planned, 1)
                    nc.tensor.matmul(ps[0:BK, 0:1], whole, ones[:, 0:1], start=True, stop=True).then_inc(planned, 1)
                    pe.wait_ge(planned, 3)
                    nc.tensor.matmul(ps[:, BANK:BANK + BK], groups_w, before[0:BK, 0:BK], start=True, stop=True)
                    nc.tensor.matmul(ps[0:BK, 2 * BANK:2 * BANK + 1], before[0:BK, 0:BK], groups_c,
                                     start=True, stop=True).then_inc(planned, 1)
                    pe.wait_ge(planned, 5)
                    nc.tensor.matmul(ps[0:1, 3 * BANK:4 * BANK], ones[0:BK, 0:1], begun[:, 0:BANK], start=True, stop=True)
                    nc.tensor.matmul(ps[0:1, 4 * BANK:3 * BANK + NSG], ones[0:BK, 0:1], begun[:, BANK:NSG],
                                     start=True, stop=True).then_inc(planned, 1)

        def bucket_pass():
            with nc.Block() as block:
                @block.sync
                def _(sp):
                    bv = bucketed.rearrange("(g p c) f -> g p (c f)", p=P, c=C)
                    with sp.Fori(0, NSG // SITER) as i:
                        for s in range(SITER):
                            n = i * SITER + s
                            sp.wait_ge(sum_taken, n + 1)
                            sp.dma_start(sorted_in[:, s].rearrange("p c f -> p (c f)"),
                                         bv[bass.ds(n, 1), :, :].rearrange("o p f -> p (o f)")
                                         ).then_inc(sorted_ready[s], 16)

                @block.tensor
                def _(pe):
                    with pe.Fori(0, NSG // SITER) as i:
                        for s in range(SITER):
                            pe.wait_ge(onehot_made, i * SITER + s + 1)
                            for c in range(C):
                                ins = nc.tensor.matmul(ps[0:D, s * BANK:s * BANK + P], sorted_in[:, s, c, 0:D],
                                                       onehot_s[:, s, c, :], start=(c == 0), stop=(c == C - 1))
                            ins.then_inc(sum_ready, 1)

                @block.vector
                def _(dve):
                    def place_onehot(i, s):
                        dve.wait_ge(sorted_ready[s], i * 16 + 16)
                        nc.vector.tensor_tensor(onehot_s[:, s], iota[:, :].unsqueeze(1).to_broadcast([P, C, P]),
                                                sorted_in[:, s, :, D:DM].to_broadcast([P, C, P]),
                                                ALU.is_equal).then_inc(onehot_made, 1)

                    def body(i, last):
                        for s in range(SITER):
                            if s + 1 < SITER:
                                place_onehot(i, s + 1)
                            elif not last:
                                place_onehot(i + 1, 0)
                            n = i * SITER + s
                            node = dve.value_load(base_s[0:1, bass.ds(n, 1)], min_val=0, max_val=NP - P)
                            at = agg[:, bass.ds(node, P)]
                            dve.wait_ge(sum_ready, n + 1)
                            dve.wait_ge(sum_taken, n + SITER)
                            nc.vector.tensor_tensor(at, at, ps[0:D, s * BANK:s * BANK + P], ALU.add).then_inc(sum_taken, 1)

                    dve.sem_inc(sum_taken, SITER)
                    place_onehot(0, 0)
                    with dve.Fori(0, NSG // SITER - 1) as i:
                        body(i, False)
                    body(NSG // SITER - 1, True)
                    dve.wait_ge(sum_taken, NSG + SITER)
            clear_pass_sems()

        round_sem = sem("round_sem")

        def load_windows(dst_from, base_from, k):
            with nc.Block() as block:
                @block.sync
                def _(sp):
                    sp.dma_start(dstloc[:, :], dst_from).then_inc(round_sem, 16)
                    sp.dma_start(base[:, :], base_from).then_inc(round_sem, 16)
                    sp.wait_ge(round_sem, 32)
            with nc.Block() as block:
                @block.sync
                def _(sp):
                    sp.sem_clear(round_sem)

        def if_missed():
            return nc.values_load(miss_i[0:1, 0:1], engines=list(nc.engines), min_val=0, max_val=E) > 0

        def further_rounds(one_pass):
            with nc.If(if_missed()):
                nc.all_engine_barrier()
                load_windows(dst_missed, base_missed, 0)
                with nc.Fori(0, ROUNDS) as _k:
                    with nc.Block() as block:
                        @block.vector
                        def _(dve):
                            nc.vector.tensor_scalar(dstloc[:, :], dstloc[:, :], -float(W), None, ALU.add)
                            nc.vector.tensor_scalar(base[:, :], base[:, :], float(W), None, ALU.add)
                    one_pass()
                load_windows(dst_main, base_main, 1)

        def center(frm, to):
            with nc.Block() as block:
                @block.vector
                def _(dve):
                    link(dve, nc.vector.tensor_reduce(mean[:, :], frm[:, :, :], axis=AX.X, op=ALU.add))
                    link(dve, nc.vector.tensor_scalar(mean[:, :], mean[:, :], 1.0 / D, None, ALU.mult))
                    link(dve, nc.vector.tensor_tensor(to[:, :, :], frm[:, :, :],
                                                      mean[:, :].unsqueeze(2).to_broadcast([P, TILES, D]), ALU.subtract))
                    link(dve, nc.vector.tensor_tensor(scratch, to[:, :, :], to[:, :, :], ALU.mult))
                    link(dve, nc.vector.tensor_reduce(var[:, :], scratch, axis=AX.X, op=ALU.add))
                    link(dve, nc.vector.tensor_scalar(var[:, :], var[:, :], 1.0 / D, EPS, ALU.mult, ALU.add))
            with nc.Block() as block:
                @block.scalar
                def _(act):
                    nc.scalar.activation(rstd[:, :], var[:, :], ACT.Sqrt)
            with nc.Block() as block:
                @block.vector
                def _(dve):
                    nc.vector.reciprocal(rstd[:, :], rstd[:, :])

        def build(layer, centred):
            rel = layer < LAYERS
            last = 2
            width = R * D if rel else D
            to_dram = table.rearrange("(n r) h -> n (r h)", r=R) if rel else wxh
            with nc.Block() as block:
                if rel:
                    @block.sync
                    def _(sp):
                        load(sp, wrel_sb[:, :, :], w_rel[layer].rearrange("r i o -> i r o"))
                        sp.wait_ge(loaded, loads[0])
            with nc.Block() as block:
                @block.scalar
                def _(act):
                    act.sem_inc(evac_s, 2)
                    with act.Fori(0, TILES // 2) as i:
                        for k in range(2):
                            t = i * 2 + k
                            if centred:
                                act.wait_ge(tile_feat, t + 1)
                                nc.scalar.activation(rows_in[:, k, :], centred[:, bass.ds(t, 1), :].rearrange(
                                    "p o d -> p (o d)"), ACT.Relu, scale=rstd[:, bass.ds(t, 1)]).then_inc(tile_in, 1)
                            else:
                                act.wait_ge(evac_v, t + 1)
                                nc.scalar.activation(feat[0:D, k, :], agg[:, bass.ds(t * P, P)],
                                                     ACT.Relu).then_inc(tile_feat, 1)
                            if rel:
                                act.wait_ge(tile_prod, t + 1)
                                act.wait_ge(tile_stored[k], i * 16 + 16)
                                nc.scalar.copy(rel_out[:, k, BANK:2 * BANK],
                                               bank(2 * k + 1)).then_inc(evac_s, 1)

                @block.vector
                def _(dve):
                    dve.sem_inc(evac_v, 2)
                    if centred:
                        dve.sem_inc(tile_feat, 2)
                    with dve.Fori(0, TILES // 2) as i:
                        for k in range(2):
                            t = i * 2 + k
                            if centred:
                                dve.wait_ge(tile_turned, t + 1)
                                dve.wait_ge(evac_v, t + 2)
                                nc.vector.tensor_copy(feat[0:D, k, :], ps[0:D, (6 + k) * BANK:(6 + k) * BANK + P]
                                                      ).then_inc(tile_feat, 1)
                            dve.wait_ge(tile_prod, t + 1)
                            dve.wait_ge(tile_stored[k], i * 16 + 16)
                            nc.vector.tensor_copy(rel_out[:, k, 0:min(width, BANK)],
                                                  bank(2 * k, min(width, BANK)))
                            if rel:
                                start = ps[0:D, (4 + k) * BANK:(4 + k) * BANK + P]
                            else:
                                dve.wait_ge(tile_feat, t + 3)
                                start = feat[0:D, k, :]
                            nc.vector.tensor_copy(agg[:, bass.ds(t * P, P)], start).then_inc(evac_v, 1)

                @block.tensor
                def _(pe):
                    ahead = 2 if centred else 0
                    with pe.Fori(0, TILES // 2) as i:
                        for k in range(2):
                            t = i * 2 + k
                            if centred:
                                pe.wait_ge(tile_in, t + 1)
                                nc.tensor.sem_inc(pe_go, 1)
                                nc.tensor.transpose(ps[0:D, (6 + k) * BANK:(6 + k) * BANK + P], rows_in[:, k, :],
                                                    ident[:, :]).then_inc(tile_turned, 1)
                            pe.wait_ge(tile_feat, t + 1 + ahead)
                            pe.wait_ge(evac_v, t + 1)
                            if rel:
                                pe.wait_ge(evac_s, t + 1)
                                for b in range(2):
                                    nc.tensor.matmul(bank(2 * k + b), feat[0:D, k, :],
                                                     wrel_sb[:, :, :].rearrange("i r o -> i (r o)")[:, b * BANK:(b + 1) * BANK],
                                                     start=True, stop=True)
                                nc.tensor.matmul(ps[0:D, (4 + k) * BANK:(4 + k) * BANK + P], wroot_sb[:, layer, :],
                                                 feat[:, k, :], start=True, stop=True).then_inc(tile_prod, 1)
                            else:
                                nc.tensor.matmul(bank(2 * k, D), feat[:, k, :], wl_t[:, :],
                                                 start=True, stop=True).then_inc(tile_prod, 1)

                @block.sync
                def _(sp):
                    for k in range(2):
                        sp.sem_inc(tile_stored[k], 16)
                    with sp.Fori(0, TILES // 2) as i:
                        for k in range(2):
                            t = i * 2 + k
                            sp.wait_ge(evac_v, t + 3)
                            if rel:
                                sp.wait_ge(evac_s, t + 3)
                            sp.dma_start(to_dram[bass.ds(t * P, P), :], rel_out[:, k, 0:width]
                                         ).then_inc(tile_stored[k], 16)
                    for k in range(2):
                        sp.wait_ge(tile_stored[k], 16 + 16 * (TILES // 2))
            clear_pass_sems()

        def rows_of_agg(to, plus):
            with nc.Block() as block:
                @block.scalar
                def _(act):
                    with act.Fori(0, TILES // 2) as i:
                        for k in range(2):
                            t = i * 2 + k
                            act.wait_ge(evac_v, t + 1)
                            nc.scalar.copy(feat[0:D, k, :], agg[:, bass.ds(t * P, P)]).then_inc(tile_feat, 1)

                @block.tensor
                def _(pe):
                    with pe.Fori(0, TILES // 2) as i:
                        for k in range(2):
                            t = i * 2 + k
                            pe.wait_ge(tile_feat, t + 1)
                            nc.tensor.sem_inc(pe_go, 1)
                            nc.tensor.transpose(bank(k, D), feat[0:D, k, :], ident[0:D, 0:D]).then_inc(tile_turned, 1)

                @block.vector
                def _(dve):
                    dve.sem_inc(evac_v, 2)
                    with dve.Fori(0, TILES // 2) as i:
                        for k in range(2):
                            t = i * 2 + k
                            dst_ap = to[:, bass.ds(t, 1), :].rearrange("p o d -> p (o d)")
                            dve.wait_ge(tile_turned, t + 1)
                            if plus is None:
                                ins = nc.vector.tensor_copy(dst_ap, bank(k, D))
                            else:
                                ins = nc.vector.tensor_tensor(dst_ap, plus[:, bass.ds(t, 1), :].rearrange(
                                    "p o d -> p (o d)"), bank(k, D), ALU.add)
                            ins.then_inc(evac_v, 1)
            clear_pass_sems()

        def copy_norms():
            with nc.Block() as block:
                @block.vector
                def _(dve):
                    link(dve, nc.vector.tensor_scalar(cnt, cnt, 1.0, None, ALU.max))
                    nc.vector.reciprocal(cnt, cnt)

        with nc.Block() as block:
            @block.vector
            def _(dve):
                nc.vector.memset(xn[:, FULL:TILES, :], 0.0).then_inc(missed, 1)

            @block.sync
            def _(sp):
                load(sp, xn[:, 0:FULL, :], x[0:FULL * P, :].rearrange("(t p) d -> p t d", p=P))
                sp.wait_ge(missed, 2)
                load(sp, xn[0:REST, FULL, :], x[FULL * P:N, :])
                sp.wait_ge(loaded, loads[0])
        center(xn, x1)
        with nc.Block() as block:
            @block.vector
            def _(dve):
                nc.vector.memset(cnt, 0.0)
                nc.vector.memset(filled[:, :], 0.0)
        count_pass()
        further_rounds(count_pass)
        copy_norms()
        for layer in range(LAYERS):
            build(layer, x1 if layer == 0 else None)
            layer_pass(layer, True)
            further_rounds(lambda: layer_pass(layer, False))
            if layer == 1:
                bucket_plan()
        rows_of_agg(x1, xn)
        center(x1, xn)
        build(LAYERS, xn)
        message_pass(True)
        with nc.If(if_missed()):
            nc.all_engine_barrier()
            message_pass(False)
        bucket_pass()
        rows_of_agg(xn, None)
        center(xn, xn)
        with nc.Block() as block:
            @block.vector
            def _(dve):
                def spread(a):
                    return a.unsqueeze(1).to_broadcast([P, TILES, D])
                y = xn[:, :, :]
                link(dve, nc.vector.tensor_tensor(y, y, rstd[:, :].unsqueeze(2).to_broadcast([P, TILES, D]), ALU.mult))
                link(dve, nc.vector.tensor_tensor(y, y, spread(gamma_sb[:, :]), ALU.mult))
                link(dve, nc.vector.tensor_tensor(y, y, spread(beta_sb[:, :]), ALU.add))
                nc.vector.tensor_tensor(y, y, x1[:, :, :], ALU.add)
        with nc.Block() as block:
            @block.sync
            def _(sp):
                sp.dma_start(out[0:FULL * P, :].rearrange("(t p) d -> p t d", p=P),
                             xn[:, 0:FULL, :]).then_inc(stored, 16)
                sp.dma_start(out[FULL * P:N, :], xn[0:REST, FULL, :]).then_inc(stored, 16)
                sp.wait_ge(stored, 112)


_INS = ['x', 'src', 'dst', 'edge_attr_64', 'edge_type_16', 'L0_gnn_W', 'L0_gnn_W_root', 'L0_gnn_bias',
        'L1_gnn_Wf1', 'L1_gnn_bf1', 'L1_gnn_Wf2', 'L1_gnn_bf2', 'L1_gnn_Wl', 'L1_gnn_bl', 'L1_gnn_gamma', 'L1_gnn_beta']
_OUTS = [((N, D), 'float32')]


def kernel(**inputs):
    import numpy as _np
    import concourse.bacc as _bacc
    from concourse import mybir as _mybir
    from concourse.bass_utils import run_bass_kernel_spmd as _run

    nc = _bacc.Bacc("TRN2", target_bir_lowering=False, num_devices=1)
    arrays, args = {}, []
    for name in _INS:
        a = _np.ascontiguousarray(inputs[name])
        arrays[f"in_{name}_dram"] = a
        args.append(nc.dram_tensor(f"in_{name}_dram", a.shape, _mybir.dt.from_np(a.dtype), kind="ExternalInput").ap())
    for i, (shape, dtype) in enumerate(_OUTS):
        dt = _mybir.dt.from_np(_np.dtype(dtype))
        args.append(nc.dram_tensor(f"out_{i}_dram", shape, dt, kind="ExternalOutput").ap())
    gnn_program(nc, *args)
    r = _run(nc, [arrays], core_ids=[0])
    return r.results[0]["out_0_dram"]
```
